# Optimizing a Trainium2 kernel written in Bass

```python
import numpy as np
import jax
import jax.numpy as jnp

def _softmax(x, axis=-1):
    return jax.nn.softmax(x, axis=axis)

def _gelu(x):
    return jax.nn.gelu(x, approximate=True)

def _silu(x):
    return jax.nn.silu(x)

def _sigmoid(x):
    return jax.nn.sigmoid(x)

def _layernorm(x, axis=-1, eps=1e-05):
    m = jnp.mean(x, axis=axis, keepdims=True)
    v = jnp.var(x, axis=axis, keepdims=True)
    return (x - m) / jnp.sqrt(v + eps)

def _scatter_add(tgt, idx, src, axis=0):
    return tgt.at[idx].add(src)

def _segment_sum(src, seg, n):
    return jax.ops.segment_sum(src, seg, n)
kernel_name = 'mk_dlrm_tower_d1_rec_r8_317a8e'

def setup_inputs(seed: int=0):
    np.random.seed(seed)
    _w = jnp.asarray

    def _rec_inputs():
        import jax
        import jax.numpy as jnp
        _tk = jax.random.key(seed)
        ids = jnp.stack([jax.random.randint(jax.random.fold_in(_tk, 200 + f), (512,), 0, v, jnp.int32) for f, v in enumerate([12500, 1250, 1000, 1250, 1000, 1000, 12500, 125000, 1000, 12500, 12500, 1250, 1250, 1000, 1000, 12500, 1000, 1250, 1000, 12500, 12500, 12500, 1000, 1000, 1250, 1000])], axis=1)
        tbl_0 = 0.05 * jax.random.normal(jax.random.fold_in(_tk, 500 + 0), (12500, 128), jnp.float32)
        tbl_1 = 0.05 * jax.random.normal(jax.random.fold_in(_tk, 500 + 1), (1250, 128), jnp.float32)
        tbl_2 = 0.05 * jax.random.normal(jax.random.fold_in(_tk, 500 + 2), (1000, 128), jnp.float32)
        tbl_3 = 0.05 * jax.random.normal(jax.random.fold_in(_tk, 500 + 3), (1250, 128), jnp.float32)
        tbl_4 = 0.05 * jax.random.normal(jax.random.fold_in(_tk, 500 + 4), (1000, 128), jnp.float32)
        tbl_5 = 0.05 * jax.random.normal(jax.random.fold_in(_tk, 500 + 5), (1000, 128), jnp.float32)
        tbl_6 = 0.05 * jax.random.normal(jax.random.fold_in(_tk, 500 + 6), (12500, 128), jnp.float32)
        tbl_7 = 0.05 * jax.random.normal(jax.random.fold_in(_tk, 500 + 7), (125000, 128), jnp.float32)
        tbl_8 = 0.05 * jax.random.normal(jax.random.fold_in(_tk, 500 + 8), (1000, 128), jnp.float32)
        tbl_9 = 0.05 * jax.random.normal(jax.random.fold_in(_tk, 500 + 9), (12500, 128), jnp.float32)
        tbl_10 = 0.05 * jax.random.normal(jax.random.fold_in(_tk, 500 + 10), (12500, 128), jnp.float32)
        tbl_11 = 0.05 * jax.random.normal(jax.random.fold_in(_tk, 500 + 11), (1250, 128), jnp.float32)
        tbl_12 = 0.05 * jax.random.normal(jax.random.fold_in(_tk, 500 + 12), (1250, 128), jnp.float32)
        tbl_13 = 0.05 * jax.random.normal(jax.random.fold_in(_tk, 500 + 13), (1000, 128), jnp.float32)
        tbl_14 = 0.05 * jax.random.normal(jax.random.fold_in(_tk, 500 + 14), (1000, 128), jnp.float32)
        tbl_15 = 0.05 * jax.random.normal(jax.random.fold_in(_tk, 500 + 15), (12500, 128), jnp.float32)
        tbl_16 = 0.05 * jax.random.normal(jax.random.fold_in(_tk, 500 + 16), (1000, 128), jnp.float32)
        tbl_17 = 0.05 * jax.random.normal(jax.random.fold_in(_tk, 500 + 17), (1250, 128), jnp.float32)
        tbl_18 = 0.05 * jax.random.normal(jax.random.fold_in(_tk, 500 + 18), (1000, 128), jnp.float32)
        tbl_19 = 0.05 * jax.random.normal(jax.random.fold_in(_tk, 500 + 19), (12500, 128), jnp.float32)
        tbl_20 = 0.05 * jax.random.normal(jax.random.fold_in(_tk, 500 + 20), (12500, 128), jnp.float32)
        tbl_21 = 0.05 * jax.random.normal(jax.random.fold_in(_tk, 500 + 21), (12500, 128), jnp.float32)
        tbl_22 = 0.05 * jax.random.normal(jax.random.fold_in(_tk, 500 + 22), (1000, 128), jnp.float32)
        tbl_23 = 0.05 * jax.random.normal(jax.random.fold_in(_tk, 500 + 23), (1000, 128), jnp.float32)
        tbl_24 = 0.05 * jax.random.normal(jax.random.fold_in(_tk, 500 + 24), (1250, 128), jnp.float32)
        tbl_25 = 0.05 * jax.random.normal(jax.random.fold_in(_tk, 500 + 25), (1000, 128), jnp.float32)
        _rk = jax.random.fold_in(_tk, 7)
        r_dense_features = -0.000520686 + 1.00062 * jax.random.normal(jax.random.fold_in(_rk, 101), (512, 128), jnp.float32)
        W_top1 = 0.0405887 * jax.random.normal(jax.random.fold_in(_tk, 801), (607, 512), jnp.float32)
        W_top2 = 0.0441942 * jax.random.normal(jax.random.fold_in(_tk, 802), (512, 256), jnp.float32)
        W_top3 = 0.0625 * jax.random.normal(jax.random.fold_in(_tk, 803), (256, 1), jnp.float32)
        b_top1 = jnp.zeros((512,), jnp.float32)
        b_top2 = jnp.zeros((256,), jnp.float32)
        return (r_dense_features, ids, tbl_0, tbl_1, tbl_2, tbl_3, tbl_4, tbl_5, tbl_6, tbl_7, tbl_8, tbl_9, tbl_10, tbl_11, tbl_12, tbl_13, tbl_14, tbl_15, tbl_16, tbl_17, tbl_18, tbl_19, tbl_20, tbl_21, tbl_22, tbl_23, tbl_24, tbl_25, W_top1, b_top1, W_top2, b_top2, W_top3)
    r_dense_features, ids, tbl_0, tbl_1, tbl_2, tbl_3, tbl_4, tbl_5, tbl_6, tbl_7, tbl_8, tbl_9, tbl_10, tbl_11, tbl_12, tbl_13, tbl_14, tbl_15, tbl_16, tbl_17, tbl_18, tbl_19, tbl_20, tbl_21, tbl_22, tbl_23, tbl_24, tbl_25, W_top1, b_top1, W_top2, b_top2, W_top3 = _rec_inputs()

    def _L0_rec_setup():
        import jax, jax.numpy as jnp
        import numpy as np
        F = 26
        B, D = (2048, 128)
        _IU0, _IU1 = np.triu_indices(F + 1, k=1)
        _IU0 = jnp.asarray(_IU0)
        _IU1 = jnp.asarray(_IU1)
        key = jax.random.key(seed)
        k1, k2 = jax.random.split(key)
        dense_features = jax.random.normal(k1, (B, D), dtype=jnp.float32)
        sparse_features = jax.random.normal(k2, (B, F, D), dtype=jnp.float32)
        return {'dense_features': dense_features, 'sparse_features': sparse_features}
    _L0_rec_all = _L0_rec_setup()
    _L0_rec_in = {k: v for k, v in _L0_rec_all.items() if k in ()}
    del _L0_rec_all
    return {'r_dense_features': r_dense_features, 'ids': ids, 'tbl_0': tbl_0, 'tbl_1': tbl_1, 'tbl_2': tbl_2, 'tbl_3': tbl_3, 'tbl_4': tbl_4, 'tbl_5': tbl_5, 'tbl_6': tbl_6, 'tbl_7': tbl_7, 'tbl_8': tbl_8, 'tbl_9': tbl_9, 'tbl_10': tbl_10, 'tbl_11': tbl_11, 'tbl_12': tbl_12, 'tbl_13': tbl_13, 'tbl_14': tbl_14, 'tbl_15': tbl_15, 'tbl_16': tbl_16, 'tbl_17': tbl_17, 'tbl_18': tbl_18, 'tbl_19': tbl_19, 'tbl_20': tbl_20, 'tbl_21': tbl_21, 'tbl_22': tbl_22, 'tbl_23': tbl_23, 'tbl_24': tbl_24, 'tbl_25': tbl_25, 'W_top1': W_top1, 'b_top1': b_top1, 'W_top2': W_top2, 'b_top2': b_top2, 'W_top3': W_top3}

def reference(r_dense_features, ids, tbl_0, tbl_1, tbl_2, tbl_3, tbl_4, tbl_5, tbl_6, tbl_7, tbl_8, tbl_9, tbl_10, tbl_11, tbl_12, tbl_13, tbl_14, tbl_15, tbl_16, tbl_17, tbl_18, tbl_19, tbl_20, tbl_21, tbl_22, tbl_23, tbl_24, tbl_25, W_top1, b_top1, W_top2, b_top2, W_top3):
    import jax
    import jax.numpy as jnp

    def _L0_rec_ref(dense_features, sparse_features):
        import jax, jax.numpy as jnp
        import numpy as np
        F = 26
        B, D = (2048, 128)
        _IU0, _IU1 = np.triu_indices(F + 1, k=1)
        _IU0 = jnp.asarray(_IU0)
        _IU1 = jnp.asarray(_IU1)
        combined = jnp.concatenate([dense_features[:, None, :], sparse_features], axis=1)
        interactions = jnp.einsum('bfd,bgd->bfg', combined, combined)
        interactions_flat = interactions[:, _IU0, _IU1]
        return jnp.concatenate([dense_features, interactions_flat], axis=1)
    e = jnp.stack([tbl_0[ids[:, 0]], tbl_1[ids[:, 1]], tbl_2[ids[:, 2]], tbl_3[ids[:, 3]], tbl_4[ids[:, 4]], tbl_5[ids[:, 5]], tbl_6[ids[:, 6]], tbl_7[ids[:, 7]], tbl_8[ids[:, 8]], tbl_9[ids[:, 9]], tbl_10[ids[:, 10]], tbl_11[ids[:, 11]], tbl_12[ids[:, 12]], tbl_13[ids[:, 13]], tbl_14[ids[:, 14]], tbl_15[ids[:, 15]], tbl_16[ids[:, 16]], tbl_17[ids[:, 17]], tbl_18[ids[:, 18]], tbl_19[ids[:, 19]], tbl_20[ids[:, 20]], tbl_21[ids[:, 21]], tbl_22[ids[:, 22]], tbl_23[ids[:, 23]], tbl_24[ids[:, 24]], tbl_25[ids[:, 25]]], axis=1)
    z = _L0_rec_ref(r_dense_features, e)
    z = z.reshape(z.shape[0], -1)
    h = jnp.concatenate([z, r_dense_features], axis=1)
    h = jnp.maximum(h @ W_top1 + b_top1, 0.0)
    h = jnp.maximum(h @ W_top2 + b_top2, 0.0)
    y = h @ W_top3
    return y

_drawn_inputs = setup_inputs


def setup_inputs(seed=0):
    import zlib

    import numpy as np

    out = dict(_drawn_inputs(seed))
    spreads = {'b_top1': (0.0, 0.1), 'b_top2': (0.0, 0.1)}
    factors = {}
    for name, (base, spread) in spreads.items():
        noise = np.random.default_rng([zlib.crc32(name.encode()), seed]).standard_normal(out[name].shape)
        drawn = base * np.exp(spread * noise) if base else spread * noise
        out[name] = jnp.asarray(drawn.astype(out[name].dtype))
    for name, factor in factors.items():
        out[name] = (out[name] * factor).astype(out[name].dtype)
    return out
```

```python
import concourse.bass as bass
from concourse import mybir
from contextlib import ExitStack
import numpy as np

BATCH, FEATURES, DIM = 512, 27, 128
TABLES = FEATURES - 1
HIDDEN1, HIDDEN2 = 512, 256
TILE = 128
TILES = BATCH // TILE
QUAD = 32
GROUP = 4
GROUPS = [list(range(g, min(g + GROUP, FEATURES))) for g in range(0, FEATURES, GROUP)]
RECTS = [(1, 0, 14, 14, 13), (1, 0, 7, 7, 7), (1, 14, 7, 21, 6), (3, 0, 3, 3, 4), (3, 0, 2, 1, 2), (3, 3, 3, 4, 3), (1, 21, 5, 22, 5)]
STEP = 7
ROWS = sum(r[0] * r[2] * r[4] for r in RECTS)
KT = [(k, min(128, ROWS - k)) for k in range(0, ROWS, 128)]


def dlrm(nc, dense, ids, tables, w1, b1, w2, b2, w3, out):
    fp32 = mybir.dt.float32
    ALU = mybir.AluOpType
    ACT = mybir.ActivationFunctionType
    H1 = HIDDEN1 // 128
    H2 = HIDDEN2 // 128
    NK = len(KT) + 2
    ctx = ExitStack()
    with ctx:
        sb = lambda n, s, d=fp32: ctx.enter_context(nc.sbuf_tensor(n, s, d))
        pb = lambda n, s, d=fp32: ctx.enter_context(nc.psum_tensor(n, s, d))
        sem = lambda n: ctx.enter_context(nc.semaphore(n))
        ids_sb = sb("ids_sb", [128, TILES, TABLES], mybir.dt.int32)
        rows = sb("rows", [128, TILES, FEATURES, DIM])
        ident = sb("ident", [128, 128])
        ones = sb("ones", [128, 128])
        xT = sb("xT", [128, TILE, QUAD])
        dT = sb("dT", [128, TILE])
        gT = sb("gT", [128, FEATURES, QUAD])
        zc = sb("zc", [128, ROWS])
        zT = sb("zT", [128, len(KT), TILE])
        w1_sb = sb("w1_sb", [128, NK, HIDDEN1])
        wd = sb("wd", [128, HIDDEN1])
        w2_sb = sb("w2_sb", [128, H1, HIDDEN2])
        w3_sb = sb("w3_sb", [128, H2])
        b1_sb = sb("b1_sb", [128, H1])
        b2_sb = sb("b2_sb", [128, H2])
        h1 = sb("h1", [128, H1, TILE])
        h2 = sb("h2", [128, H2, TILE])
        y = sb("y", [1, TILES, TILE])
        pX = [pb(f"pX{i}", [128, GROUP, 128]) for i in range(2)]
        pG = pb("pG", [128, 2, 512])
        pZ = pb("pZ", [128, len(KT), TILE])
        pH = pb("pH", [128, H1, TILE])
        pH2 = pb("pH2", [128, H2, TILE])
        pY = pb("pY", [1, TILE])
        s_ids = sem("s_ids"); s_dense = sem("s_dense"); s_w = sem("s_w"); s_cst = sem("s_cst")
        s_rows = [[sem(f"s_rows{t}_{g}") for g in range(len(GROUPS))] for t in range(TILES)]
        s_tp = sem("s_tp"); s_xa = sem("s_xa"); s_xd = sem("s_xd"); s_pad = sem("s_pad")
        s_gram = sem("s_gram"); s_gt = sem("s_gt"); s_zp = sem("s_zp"); s_zc = sem("s_zc")
        s_h1p = sem("s_h1p"); s_h1 = sem("s_h1"); s_h2p = sem("s_h2p"); s_h2 = sem("s_h2")
        s_yp = sem("s_yp"); s_y = sem("s_y"); s_out = sem("s_out"); s_wd = sem("s_wd"); s_id = sem("s_id")
        s_gtd = sem("s_gtd")
        NG = len(GROUPS)

        def gT_rect(n, f0, nf, g0, ng):
            a = gT[:, f0:f0 + nf, g0:g0 + ng]
            p, fa, ga = a.ap
            return bass.AP(a.tensor, a.offset, [p, [STEP * (QUAD + 1), n], fa, ga])
        block = ctx.enter_context(nc.Block())

        @block.sync
        def _(sp):
            sp.dma_start(ids_sb[:], ids.rearrange("(p t) f -> p t f", t=TILES)).then_inc(s_ids, 16)
            sp.dma_start(rows[:, :, 0, :], dense.rearrange("(p t) d -> p t d", t=TILES)).then_inc(s_dense, 16)
            sp.dma_start(w1_sb[:], w1).then_inc(s_w, 16)
            sp.dma_start(w2_sb[:], w2.rearrange("(k p) n -> p k n", p=128)).then_inc(s_w, 16)
            with nc.allow_non_contiguous_dma(reason="small"):
                sp.dma_start(w3_sb[:], w3.rearrange("(k p) o -> p (k o)", p=128)).then_inc(s_w, 16)
                sp.dma_start(b1_sb[:], b1.rearrange("(k p) -> p k", p=128)).then_inc(s_w, 16)
                sp.dma_start(b2_sb[:], b2.rearrange("(k p) -> p k", p=128)).then_inc(s_w, 16)
            sp.wait_ge(s_y, TILES)
            sp.dma_start(out.rearrange("(p t) o -> o t p", t=TILES), y[:]).then_inc(s_out, 16) if False else None
            with nc.allow_non_contiguous_dma(reason="small"):
                sp.dma_start(out.rearrange("(p t) o -> o t p", t=TILES), y[:]).then_inc(s_out, 16)
            sp.wait_ge(s_out, 16)

        @block.gpsimd
        def _(pool):
            pool.memset(ones[:], 1.0).then_inc(s_cst, 1)
            pool.wait_ge(s_cst, 1)
            pool.affine_select(out=ident[:], in_=ones[:], compare_op=ALU.is_equal, fill=0.0, base=0,
                               pattern=[[-1, 128]], channel_multiplier=1).then_inc(s_id, 1)
            pool.wait_ge(s_ids, 16)
            for t in range(TILES):
                for g, group in enumerate(GROUPS):
                    for f in group:
                        if f:
                            pool.indirect_dma_start(
                                out=rows[:, t, f, :], out_offset=None, in_=tables[f - 1],
                                in_offset=bass.IndirectOffsetOnAxis(ap=ids_sb[:, t, f - 1:f], axis=0)).then_inc(s_rows[t][g], 16)

        @block.vector
        def _(dve):
            dve.memset(xT[:, :, FEATURES:QUAD], 0.0).then_inc(s_pad, 1)
            dve.wait_ge(s_w, 80)
            nc.vector.tensor_add(wd[:], w1_sb[:, NK - 2, :], w1_sb[:, NK - 1, :]).then_inc(s_wd, 1)
            for t in range(TILES):
                for g, group in enumerate(GROUPS):
                    if g % 2 == 1:
                        dve.wait_ge(s_tp, NG * t + g + 1)
                        if t:
                            dve.wait_ge(s_gram, t)
                        n = len(group)
                        nc.vector.tensor_copy(xT[:, :, group[0]:group[0] + n], pX[g % 2][:, 0:n, :].rearrange("p f b -> p b f")).then_inc(s_xd, 1)
                    else:
                        pass
                dve.wait_ge(s_gram, t + 1)
                if t:
                    dve.wait_ge(s_zp, t)
                nc.vector.transpose(gT[:], pG[:, :, 0:16 * FEATURES].rearrange("p h (m g) -> p g h m", g=FEATURES)).then_inc(s_gtd, 1)
                dve.wait_ge(s_gtd, t + 1)
                at = 0
                for n, f0, nf, g0, ng in RECTS:
                    size = nf * ng
                    src = gT_rect(n, f0, nf, g0, ng)
                    last = nc.vector.tensor_copy(zc[:, at:at + n * size].rearrange("p (n f g) -> p n f g", n=n, g=ng), src)
                    at += n * size
                last.then_inc(s_gt, 1)

        @block.scalar
        def _(act):
            for t in range(TILES):
                for g, group in enumerate(GROUPS):
                    if g % 2 == 0:
                        act.wait_ge(s_tp, NG * t + g + 1)
                        if t:
                            act.wait_ge(s_gram, t)
                        n = len(group)
                        nc.scalar.copy(xT[:, :, group[0]:group[0] + n], pX[g % 2][:, 0:n, :].rearrange("p f b -> p b f")).then_inc(s_xa, 1)
                        if g == 0:
                            if t:
                                act.wait_ge(s_h1p, t)
                            nc.scalar.copy(dT[:], pX[0][:, 0, :]).then_inc(s_xa, 1)
                act.wait_ge(s_zp, t + 1)
                for j, (_, k) in enumerate(KT):
                    nc.scalar.copy(zT[0:k, j, :], pZ[0:k, j, :]).then_inc(s_zc, 1)
                act.wait_ge(s_h1p, t + 1)
                for n in range(H1):
                    nc.scalar.activation(h1[:, n, :], pH[:, n, :], ACT.Relu, bias=b1_sb[:, n:n + 1]).then_inc(s_h1, 1)
                act.wait_ge(s_h2p, t + 1)
                for n in range(H2):
                    nc.scalar.activation(h2[:, n, :], pH2[:, n, :], ACT.Relu, bias=b2_sb[:, n:n + 1]).then_inc(s_h2, 1)
                act.wait_ge(s_yp, t + 1)
                nc.scalar.copy(y[:, t, :], pY[:]).then_inc(s_y, 1)

        @block.tensor
        def _(pe):
            pe.wait_ge(s_id, 1)
            pe.wait_ge(s_dense, 16)
            for t in range(TILES):
                for g, group in enumerate(GROUPS):
                    pe.wait_ge(s_rows[t][g], 16 * sum(1 for f in group if f))
                    if g % 2 == 0 and (t or g):
                        pe.wait_ge(s_xa, 5 * t + (g // 2 + 1 if g else 0))
                    if g % 2 == 1 and (t or g > 1):
                        pe.wait_ge(s_xd, 3 * t + g // 2)
                    for i, f in enumerate(group):
                        last = nc.tensor.transpose(pX[g % 2][:, i, :], rows[:, t, f, :], ident[:])
                    last.then_inc(s_tp, 1)
                pe.wait_ge(s_xa, (t + 1) * 5)
                pe.wait_ge(s_xd, (t + 1) * 3)
                if t == 0:
                    pe.wait_ge(s_pad, 1)
                if t:
                    pe.wait_ge(s_gt, t)
                for m in range(QUAD):
                    for s in range(4):
                        b = QUAD * s + m
                        c = (m % 16) * FEATURES
                        last = nc.tensor.matmul(pG[QUAD * s:QUAD * s + QUAD, m // 16, c:c + FEATURES], xT[:, b, :], xT[:, b, 0:FEATURES], start=True, stop=True)
                last.then_inc(s_gram, 1)
                pe.wait_ge(s_gt, t + 1)
                if t:
                    pe.wait_ge(s_zc, 3 * t)
                for j, (a, k) in enumerate(KT):
                    last = nc.tensor.transpose(pZ[0:k, j, :], zc[:, a:a + k], ident[:])
                last.then_inc(s_zp, 1)
                if t == 0:
                    pe.wait_ge(s_wd, 1)
                    pe.wait_ge(s_w, 80)
                pe.wait_ge(s_zc, 3 * (t + 1))
                if t:
                    pe.wait_ge(s_h1, H1 * t)
                for n in range(H1):
                    c = slice(n * 128, n * 128 + 128)
                    nc.tensor.matmul(pH[:, n, :], wd[:, c], dT[:], start=True, stop=False)
                    for j, (_, k) in enumerate(KT):
                        last = nc.tensor.matmul(pH[:, n, :], w1_sb[0:k, j, c], zT[0:k, j, :], start=False, stop=j == len(KT) - 1)
                last.then_inc(s_h1p, 1)
                pe.wait_ge(s_h1, H1 * (t + 1))
                if t:
                    pe.wait_ge(s_h2, H2 * t)
                for n in range(H2):
                    for k in range(H1):
                        last = nc.tensor.matmul(pH2[:, n, :], w2_sb[:, k, n * 128:n * 128 + 128], h1[:, k, :], start=k == 0, stop=k == H1 - 1)
                last.then_inc(s_h2p, 1)
                pe.wait_ge(s_h2, H2 * (t + 1))
                if t:
                    pe.wait_ge(s_y, t)
                for k in range(H2):
                    last = nc.tensor.matmul(pY[:], w3_sb[:, k:k + 1], h2[:, k, :], start=k == 0, stop=k == H2 - 1)
                last.then_inc(s_yp, 1)


def lay_w1(w):
    laid = np.zeros((128 * len(KT), HIDDEN1), w.dtype)
    first = [DIM]
    for f in range(FEATURES):
        first.append(first[f] + FEATURES - 1 - f)
    at = 0
    for n, f0, nf, g0, ng in RECTS:
        for k in range(n):
            for f in range(f0 + k * STEP, f0 + k * STEP + nf):
                for g in range(g0 + k * STEP, g0 + k * STEP + ng):
                    if f < g:
                        laid[at] = w[first[f] + g - f - 1]
                    at += 1
    row = first[-1]
    laid = np.concatenate([laid.reshape(len(KT), 128, HIDDEN1).transpose(1, 0, 2), np.zeros((128, 2, HIDDEN1), w.dtype)], 1)
    laid[:, -2] = w[0:DIM]
    laid[:, -1] = w[row:row + DIM]
    return laid


def kernel(**inputs):
    import concourse.bacc as bacc
    from concourse.bass_utils import run_bass_kernel_spmd
    nc = bacc.Bacc("TRN2", target_bir_lowering=False, num_devices=1)
    arrays = {n: np.ascontiguousarray(a) for n, a in inputs.items()}
    arrays["W_top1"] = lay_w1(arrays["W_top1"])
    ap = {n: nc.dram_tensor(n, a.shape, mybir.dt.from_np(a.dtype), kind="ExternalInput").ap() for n, a in arrays.items()}
    out = nc.dram_tensor("y_out", (BATCH, 1), mybir.dt.float32, kind="ExternalOutput").ap()
    dlrm(nc, ap["r_dense_features"], ap["ids"], [ap[f"tbl_{i}"] for i in range(TABLES)], ap["W_top1"], ap["b_top1"],
         ap["W_top2"], ap["b_top2"], ap["W_top3"], out)
    r = run_bass_kernel_spmd(nc, [arrays], core_ids=[0])
    return r.results[0]["y_out"]
```

```python
import concourse.bass as bass
from concourse import mybir
from contextlib import ExitStack
import numpy as np

BATCH, DIM = 512, 128
TABLES = 26
SLOTS = TABLES + 1
HIDDEN1, HIDDEN2 = 512, 256
H1, H2 = HIDDEN1 // 128, HIDDEN2 // 128
TILE = 128
TILES = BATCH // TILE
RAW_BUFFERS = 3
BEFORE_GRAM = 7
QUAD = 32

SMALL, CHUNKS = 1000, 8
SMALL_P = SMALL // CHUNKS
SMALL_16 = SMALL_P // 16 * 16
ONEHOT = [2, 4, 5, 8, 13, 14, 16, 18, 22, 23]
GATHERED = [i for i in range(TABLES) if i not in ONEHOT]
LOOKED_UP = BATCH - TILE
DVE_CHUNKS = 6
SLOT_FEATURE = [0] + [i + 1 for i in GATHERED + ONEHOT]
FIRST_ONEHOT = 1 + len(GATHERED)


def slot_groups(t):
    end = SLOTS if t == 0 else FIRST_ONEHOT
    return [list(range(s, min(s + 4, end))) for s in range(0, end, 4)]


TURNS = [(t, g) for t in range(TILES) for g in range(len(slot_groups(t)))]


def turns_through(t):
    return sum(1 for u, _ in TURNS if u <= t)


STEP = 7
RECTS = [(1, 0, 14, 14, 13), (1, 0, 7, 7, 7), (1, 14, 7, 21, 6), (3, 0, 3, 3, 4), (3, 0, 2, 1, 2),
         (3, 3, 3, 4, 3), (1, 21, 5, 22, 5)]
PACKED = sum(r[0] * r[2] * r[4] for r in RECTS)
NKT = -(-PACKED // 128)
KROWS = -(-PACKED // NKT)


def schedule():
    order = [("prepare", 0), ("high", 0), ("prepare", 1)]
    ready, looked = 2, 0

    def look():
        nonlocal ready, looked
        if looked + 1 < len(ONEHOT):
            order.append(("high", looked + 1))
        order.append(("look", looked))
        looked += 1
        if ready < len(ONEHOT):
            order.append(("prepare", ready))
            ready += 1

    for g in range(len(slot_groups(0))):
        if looked < BEFORE_GRAM:
            look()
        order.append(("turn", 0, g))
    order.append(("gram", 0))
    for t in range(1, TILES):
        behind = [[("pairs", t - 1)], [("layer1", t - 1)], [("layer2", t - 1)], [("layer3", t - 1)]]
        if t == TILES - 1:
            late = [behind.pop(-2)[0], behind.pop(-1)[0]]
        order.append(("pack", t - 1))
        if t == 1:
            look()
        for g in range(len(slot_groups(t))):
            order.append(("turn", t, g))
            if t == 1 and looked < len(ONEHOT) and g >= 1:
                look()
            if g >= 1 and behind:
                order += behind.pop(0)
        for steps in behind:
            order += steps
        while looked < len(ONEHOT):
            look()
        order.append(("gram", t))
    t = TILES - 1
    return order + late + [("pack", t), ("pairs", t), ("layer1", t), ("layer2", t), ("layer3", t)]


SCHEDULE = schedule()


def done_before(step, kind):
    return sum(1 for s in SCHEDULE[:SCHEDULE.index(step)] if s[0] == kind)


def dlrm(nc, dense, ids, ids_small, tables, w1, b1, w2, b2, w3, out):
    fp32, fp32r, i32 = mybir.dt.float32, mybir.dt.float32r, mybir.dt.int32
    ALU = mybir.AluOpType
    ACT = mybir.ActivationFunctionType
    NO = len(ONEHOT)
    ctx = ExitStack()
    with ctx:
        sb = lambda n, s, d=fp32: ctx.enter_context(nc.sbuf_tensor(n, s, d))
        pb = lambda n, s, d=fp32: ctx.enter_context(nc.psum_tensor(n, s, d))
        sem = lambda n: ctx.enter_context(nc.semaphore(n))
        ids_sb = sb("ids_sb", [128, TILES, TABLES], i32)
        idb = sb("idb", [128, NO, LOOKED_UP], i32)
        rowid = sb("rowid", [128, CHUNKS])
        rows = sb("rows", [128, 2, SLOTS, DIM])
        dense_sb = sb("dense_sb", [128, TILES, DIM])
        raw = sb("raw", [SMALL_P, RAW_BUFFERS, CHUNKS * DIM])
        cut = sb("cut", [SMALL_P, 2, CHUNKS * DIM])
        high = sb("high", [SMALL_P, 2, CHUNKS * DIM], fp32r)
        low = sb("low", [SMALL_P, 2, CHUNKS * DIM], fp32r)
        hot = sb("hot", [SMALL_P, 2, CHUNKS, LOOKED_UP], fp32r)
        apart = sb("apart", [SMALL_P, CHUNKS - DVE_CHUNKS, LOOKED_UP])
        ident = sb("ident", [128, 128])
        ones = sb("ones", [128, 128])
        xT = sb("xT", [128, BATCH, SLOTS])
        gT = sb("gT", [128, SLOTS, QUAD])
        zc = sb("zc", [128, NKT * KROWS])
        zT = sb("zT", [KROWS, NKT, TILE])
        w1_sb = sb("w1_sb", [128, NKT + 2, HIDDEN1])
        w2_sb = sb("w2_sb", [128, H1, HIDDEN2])
        w3_sb = sb("w3_sb", [128, H2])
        b1_sb = sb("b1_sb", [128, H1])
        b2_sb = sb("b2_sb", [128, H2])
        h1 = sb("h1", [128, H1, TILE])
        h2 = sb("h2", [128, H2, TILE])
        y = sb("y", [1, TILE, TILES])
        pX = pb("pX", [128, 2, 4, 128])
        pG = pb("pG", [128, 2, 512])
        pH = pb("pH", [128, 2, 512])
        pH2 = pb("pH2", [128, 512])
        pOZ = pb("pOZ", [128, 512])
        look_ps = pOZ[:, 0:LOOKED_UP]
        pairs_ps = pOZ[0:KROWS, 0:NKT * TILE].rearrange("p (k b) -> p k b", k=NKT)
        h1_ps = [pH[:, n % 2, (n // 2) * TILE:(n // 2 + 1) * TILE] for n in range(H1)]
        h2_ps = [pH2[:, 0:TILE], pH[:, 0, 2 * TILE:3 * TILE]]
        y_ps = pH2[0:1, TILE:2 * TILE]

        s_ids = sem("ids_loaded"); s_idb = [sem(f"ids_small_loaded{n}") for n in range(0, -(-NO // 3))]; s_dense = sem("dense_loaded")
        s_w = sem("weights_loaded"); s_tbl = [sem(f"table_loaded{k}") for k in range(RAW_BUFFERS)]
        s_rows = [[sem(f"rows_gathered{t}_{g}") for g in range(len(slot_groups(0)))] for t in range(2)]
        s_ones = sem("ones_set"); s_const = sem("constants_set"); s_pg = sem("gram_psum_cleared")
        s_cut = sem("table_cut"); s_low = sem("low_ready"); s_high = sem("high_ready"); s_hot = sem("hot_ready_by_dve"); s_hota = sem("hot_ready_by_act"); s_apart = sem("row_distance_ready")
        s_oh = sem("lookup_done"); s_ohx = sem("lookup_copied")
        s_tp = sem("rows_turned"); s_xa = sem("turned_copied")
        s_gram = sem("gram_done"); s_gt = sem("gram_turned"); s_zc = sem("pairs_packed")
        s_zp = sem("pairs_turned"); s_zt = sem("pairs_copied"); s_zpad = sem("pairs_padded"); s_wd = sem("dense_weights_added")
        s_h1p = sem("layer1_done"); s_h1 = sem("layer1_relu"); s_h2p = sem("layer2_done"); s_h2 = sem("layer2_relu")
        s_yp = sem("layer3_done"); s_y = sem("y_copied"); s_out = sem("out_stored")

        def rect_of(copies, a0, na, b0, nb):
            one = gT[:, a0:a0 + na, b0:b0 + nb]
            p, a, b = one.ap
            return bass.AP(one.tensor, one.offset, [p, [STEP * (QUAD + 1), copies], a, b])

        def load_small_ids(queue, n):
            some = ids_small[3 * n:min(3 * n + 3, NO)]
            queue.dma_start(idb[:, 3 * n:min(3 * n + 3, NO), :], some.rearrange("(o k) b -> o k b", o=1).to_broadcast([128, *some.shape])
                            ).then_inc(s_idb[n], 16)

        def load_table(queue, k):
            table = tables[ONEHOT[k]].rearrange("(p c) d -> p (c d)", c=CHUNKS)
            queue.dma_start(raw[0:SMALL_16, k % RAW_BUFFERS, :], table[0:SMALL_16]).then_inc(s_tbl[k % RAW_BUFFERS], 16)
            queue.dma_start(raw[SMALL_16:SMALL_P, k % RAW_BUFFERS, :], table[SMALL_16:SMALL_P]).then_inc(s_tbl[k % RAW_BUFFERS], 16)
        block = ctx.enter_context(nc.Block())

        @block.sync
        def _(sp):
            sp.dma_start(ids_sb[:], ids.rearrange("(p t) f -> p t f", t=TILES)).then_inc(s_ids, 16)
            load_small_ids(sp, 0)
            load_table(sp, 1)
            sp.dma_start(dense_sb[:], dense.rearrange("(p t) d -> p t d", t=TILES)).then_inc(s_dense, 16)
            for k in range(2, NO):
                if k >= RAW_BUFFERS:
                    sp.wait_ge(s_low, k - RAW_BUFFERS + 1)
                load_table(sp, k)
                if k == 4:
                    sp.dma_start(w1_sb[:], w1).then_inc(s_w, 16)
                    sp.dma_start(w2_sb[:], w2.rearrange("(k p) n -> p k n", p=128)).then_inc(s_w, 16)
                    with nc.allow_non_contiguous_dma(reason="a column, or biases by output row: a few hundred elements"):
                        sp.dma_start(w3_sb[:], w3.rearrange("(k p) o -> p (k o)", p=128)).then_inc(s_w, 16)
                        sp.dma_start(b1_sb[:], b1.rearrange("(k p) -> p k", p=128)).then_inc(s_w, 16)
                        sp.dma_start(b2_sb[:], b2.rearrange("(k p) -> p k", p=128)).then_inc(s_w, 16)
            sp.wait_ge(s_y, TILES)
            sp.dma_start(out.rearrange("(p t) o -> o p t", t=TILES), y[:]).then_inc(s_out, 16)
            sp.wait_ge(s_out, 16)

        @block.gpsimd
        def _(pool):
            pool.iota(rowid[:], pattern=[[1, CHUNKS]], base=0, channel_multiplier=CHUNKS,
                      allow_small_or_imprecise_dtypes=True).then_inc(s_const, 1)
            pool.memset(ones[:], 1.0).then_inc(s_ones, 1)
            pool.wait_ge(s_ones, 1)
            pool.affine_select(out=ident[:], in_=ones[:], compare_op=ALU.is_equal, fill=0.0, base=0,
                               pattern=[[-1, 128]], channel_multiplier=1).then_inc(s_const, 1)
            pool.wait_ge(s_ids, 16)
            for t, g in TURNS:
                if t >= 2:
                    pool.wait_ge(s_tp, TURNS.index((t - 2, g)) + 1)
                for slot in slot_groups(t)[g]:
                    if slot:
                        i = SLOT_FEATURE[slot] - 1
                        pool.indirect_dma_start(
                            out=rows[:, t % 2, slot, :], out_offset=None, in_=tables[i],
                            in_offset=bass.IndirectOffsetOnAxis(ap=ids_sb[:, t, i:i + 1], axis=0)).then_inc(s_rows[t % 2][g], 16)

        @block.vector
        def _(dve):
            def split(k):
                dve.wait_ge(s_tbl[k % RAW_BUFFERS], 32 * (k // RAW_BUFFERS + 1))
                if k >= 2:
                    dve.wait_ge(s_high, k - 1)
                    dve.wait_ge(s_oh, k - 1)
                nc.vector.tensor_scalar(cut[:, k % 2, :].bitcast(i32), raw[:, k % RAW_BUFFERS, :].bitcast(i32), -4096, None,
                                        ALU.bitwise_and).then_inc(s_cut, 1)
                dve.wait_ge(s_cut, k + 1)
                nc.vector.tensor_sub(low[:, k % 2, :], raw[:, k % RAW_BUFFERS, :], cut[:, k % 2, :]).then_inc(s_low, 1)

            def one_hot(j):
                if j == 0:
                    dve.wait_ge(s_const, 2)
                if j >= 2:
                    dve.wait_ge(s_oh, j - 1)
                dve.wait_ge(s_idb[j // 3], 16)
                for c in range(DVE_CHUNKS):
                    last = nc.vector.tensor_scalar(hot[:, j % 2, c, :], idb[0:SMALL_P, j, :],
                                                   rowid[0:SMALL_P, c:c + 1], None, ALU.is_equal)
                last.then_inc(s_hot, 1)

            nc.vector.memset(pG[:], 0.0).then_inc(s_pg, 1)
            nc.vector.memset(zc[:, PACKED:], 0.0).then_inc(s_zpad, 1)
            for step in SCHEDULE:
                if step[0] == "prepare" and step[1] == 0:
                    one_hot(0)
                    split(0)
                elif step[0] == "prepare":
                    split(step[1])
                    one_hot(step[1])
                if step[0] == "pack":
                    t = step[1]
                    if t == 0:
                        dve.wait_ge(s_w, 80)
                        nc.vector.tensor_add(w1_sb[:, NKT, :], w1_sb[:, NKT, :], w1_sb[:, NKT + 1, :]).then_inc(s_wd, 1)
                    dve.wait_ge(s_gram, t + 1)
                    if t:
                        dve.wait_ge(s_zp, t)
                        dve.wait_ge(s_zc, t)
                    nc.vector.transpose(gT[:], pG[:, :, 0:16 * SLOTS].rearrange("p h (m g) -> p g h m", g=SLOTS)).then_inc(s_gt, 1)
                    dve.wait_ge(s_gt, t + 1)
                    at = 0
                    for rect in RECTS:
                        copies, _, na, _, nb = rect
                        size = copies * na * nb
                        last = nc.vector.tensor_copy(zc[:, at:at + size].rearrange("p (n a b) -> p n a b", n=copies, b=nb),
                                                     rect_of(*rect))
                        at += size
                    last.then_inc(s_zc, 1)

        @block.scalar
        def _(act):
            load_table(act, 0)
            for n in range(1, -(-NO // 3)):
                load_small_ids(act, n)

            def high_part(k):
                act.wait_ge(s_cut, k + 1)
                if k >= 2:
                    act.wait_ge(s_oh, k - 1)
                nc.scalar.copy(high[:, k % 2, :], cut[:, k % 2, :]).then_inc(s_high, 1)

            def one_hot(j):
                if j == 0:
                    act.wait_ge(s_const, 2)
                act.wait_ge(s_idb[j // 3], 16)
                if j:
                    act.wait_ge(s_hota, j)
                if j >= 2:
                    act.wait_ge(s_oh, j - 1)
                for c in range(DVE_CHUNKS, CHUNKS):
                    last = nc.scalar.activation(apart[:, c - DVE_CHUNKS, :], idb[0:SMALL_P, j, :], ACT.Abs,
                                                bias=rowid[0:SMALL_P, c:c + 1], scale=-1.0)
                last.then_inc(s_apart, 1)
                act.wait_ge(s_apart, j + 1)
                nc.scalar.activation(hot[:, j % 2, DVE_CHUNKS:, :], apart[:], ACT.Relu, bias=1.0, scale=-1.0).then_inc(s_hota, 1)
            for step in SCHEDULE:
                if step[0] == "look":
                    j = step[1]
                    act.wait_ge(s_oh, j + 1)
                    nc.scalar.copy(xT[:, TILE:BATCH, FIRST_ONEHOT + j], look_ps).then_inc(s_ohx, 1)
                if step[0] == "high":
                    if step[1] == 0:
                        one_hot(0)
                        high_part(0)
                    else:
                        high_part(step[1])
                        one_hot(step[1])
                if step[0] == "turn":
                    t, g = step[1:]
                    turn = TURNS.index((t, g))
                    first, n = slot_groups(t)[g][0], len(slot_groups(t)[g])
                    act.wait_ge(s_tp, turn + 1)
                    nc.scalar.copy(xT[:, t * TILE:(t + 1) * TILE, first:first + n],
                                   pX[:, turn % 2, 0:n, :].rearrange("p f b -> p b f")).then_inc(s_xa, 1)
                if step[0] == "pairs":
                    t = step[1]
                    act.wait_ge(s_zp, t + 1)
                    if t:
                        act.wait_ge(s_h1p, H1 * t)
                    nc.scalar.copy(zT[:], pairs_ps).then_inc(s_zt, 1)
                if step[0] == "layer1":
                    t = step[1]
                    if t:
                        act.wait_ge(s_h2p, H2 * t)
                    else:
                        act.wait_ge(s_w, 80)
                    for n in range(H1):
                        act.wait_ge(s_h1p, H1 * t + n + 1)
                        nc.scalar.activation(h1[:, n, :], h1_ps[n], ACT.Relu, bias=b1_sb[:, n:n + 1]).then_inc(s_h1, 1)
                if step[0] == "layer2":
                    t = step[1]
                    if t:
                        act.wait_ge(s_yp, t)
                    for n in range(H2):
                        act.wait_ge(s_h2p, H2 * t + n + 1)
                        nc.scalar.activation(h2[:, n, :], h2_ps[n], ACT.Relu, bias=b2_sb[:, n:n + 1]).then_inc(s_h2, 1)
                if step[0] == "layer3":
                    t = step[1]
                    act.wait_ge(s_yp, t + 1)
                    nc.scalar.copy(y[:, :, t], y_ps).then_inc(s_y, 1)

        @block.tensor
        def _(pe):
            def lookup(j):
                pe.wait_ge(s_hot, j + 1)
                pe.wait_ge(s_hota, j + 1)
                pe.wait_ge(s_low, j + 1)
                pe.wait_ge(s_high, j + 1)
                if j:
                    pe.wait_ge(s_ohx, j)
                if done_before(("look", j), "pairs"):
                    pe.wait_ge(s_zt, done_before(("look", j), "pairs"))
                for part in (high, low):
                    for c in range(CHUNKS):
                        last = nc.tensor.matmul(look_ps, part[:, j % 2, c * DIM:(c + 1) * DIM], hot[:, j % 2, c, :],
                                                start=part is high and c == 0, stop=part is low and c == CHUNKS - 1)
                last.then_inc(s_oh, 1)

            def turn_rows(t, g):
                turn = TURNS.index((t, g))
                if turn == 0:
                    pe.wait_ge(s_dense, 16)
                gathered = sum(1 for u in range(t % 2, t + 1, 2) for slot in slot_groups(u)[g] if slot)
                pe.wait_ge(s_rows[t % 2][g], 16 * gathered)
                if turn >= 2:
                    pe.wait_ge(s_xa, turn - 1)
                for i, slot in enumerate(slot_groups(t)[g]):
                    src = rows[:, t % 2, slot, :] if slot else dense_sb[:, t, :]
                    last = nc.tensor.transpose(pX[:, turn % 2, i, :], src, ident[:])
                last.then_inc(s_tp, 1)

            def gram(t):
                pe.wait_ge(s_xa, turns_through(t))
                if t == 0:
                    pe.wait_ge(s_pg, 1)
                else:
                    pe.wait_ge(s_ohx, NO)
                    pe.wait_ge(s_gt, t)
                for m in range(QUAD):
                    for q in range(4):
                        x = xT[:, t * TILE + QUAD * q + m, :]
                        c = (m % 16) * SLOTS
                        last = nc.tensor.matmul(pG[QUAD * q:QUAD * q + SLOTS, m // 16, c:c + SLOTS], x, x, start=True, stop=True)
                last.then_inc(s_gram, 1)

            def turn_pairs(t):
                pe.wait_ge(s_zc, t + 1)
                if t:
                    pe.wait_ge(s_zt, t)
                else:
                    pe.wait_ge(s_zpad, 1)
                if done_before(("pairs", t), "look"):
                    pe.wait_ge(s_ohx, done_before(("pairs", t), "look"))
                for k in range(NKT):
                    last = nc.tensor.transpose(pairs_ps[:, k, :], zc[:, k * KROWS:(k + 1) * KROWS], ident[:])
                last.then_inc(s_zp, 1)

            def layer1(t):
                if t == 0:
                    pe.wait_ge(s_wd, 1)
                    pe.wait_ge(s_w, 80)
                else:
                    pe.wait_ge(s_h2, H2 * t)
                    pe.wait_ge(s_h1, H1 * t)
                for n in range(2):
                    nc.tensor.matmul(h1_ps[n], w1_sb[:, NKT, n * 128:(n + 1) * 128], xT[:, t * TILE:(t + 1) * TILE, 0],
                                     start=True, stop=False)
                pe.wait_ge(s_zt, t + 1)
                for n in range(H1):
                    c = slice(n * 128, (n + 1) * 128)
                    if n >= 2:
                        pe.wait_ge(s_h1, H1 * t + n - 1)
                        nc.tensor.matmul(h1_ps[n], w1_sb[:, NKT, c], xT[:, t * TILE:(t + 1) * TILE, 0], start=True, stop=False)
                    for k in range(NKT):
                        last = nc.tensor.matmul(h1_ps[n], w1_sb[0:KROWS, k, c], zT[:, k, :], start=False, stop=k == NKT - 1)
                    last.then_inc(s_h1p, 1)

            def layer2(t):
                if t:
                    pe.wait_ge(s_y, t)
                for n, blocks in [(0, range(H1 - 1)), (1, range(H1 - 1)), (0, [H1 - 1]), (1, [H1 - 1])]:
                    for k in blocks:
                        pe.wait_ge(s_h1, H1 * t + k + 1)
                        last = nc.tensor.matmul(h2_ps[n], w2_sb[:, k, n * 128:(n + 1) * 128], h1[:, k, :], start=k == 0,
                                                stop=k == H1 - 1)
                    if k == H1 - 1:
                        last.then_inc(s_h2p, 1)

            def layer3(t):
                for k in range(H2):
                    pe.wait_ge(s_h2, H2 * t + k + 1)
                    last = nc.tensor.matmul(y_ps, w3_sb[:, k:k + 1], h2[:, k, :], start=k == 0, stop=k == H2 - 1)
                last.then_inc(s_yp, 1)

            pe.wait_ge(s_const, 2)
            for step in SCHEDULE:
                if step[0] in ("prepare", "high", "pack"):
                    continue
                {"look": lookup, "turn": turn_rows, "gram": gram, "pairs": turn_pairs, "layer1": layer1,
                 "layer2": layer2, "layer3": layer3}[step[0]](*step[1:])


def laid_w1(w):
    first = [DIM]
    for f in range(SLOTS):
        first.append(first[f] + SLOTS - 1 - f)
    laid = np.zeros((NKT * KROWS, HIDDEN1), w.dtype)
    at = 0
    for copies, a0, na, b0, nb in RECTS:
        for k in range(copies):
            for a in range(a0 + k * STEP, a0 + k * STEP + na):
                for b in range(b0 + k * STEP, b0 + k * STEP + nb):
                    if a < b:
                        f, g = sorted((SLOT_FEATURE[a], SLOT_FEATURE[b]))
                        laid[at] = w[first[f] + g - f - 1]
                    at += 1
    tiles = np.zeros((128, NKT + 2, HIDDEN1), w.dtype)
    tiles[0:KROWS, 0:NKT] = laid.reshape(NKT, KROWS, HIDDEN1).transpose(1, 0, 2)
    tiles[:, NKT] = w[0:DIM]
    tiles[:, NKT + 1] = w[first[-1]:first[-1] + DIM]
    return tiles


def kernel(**inputs):
    import concourse.bacc as bacc
    from concourse.bass_utils import run_bass_kernel_spmd
    nc = bacc.Bacc("TRN2", target_bir_lowering=False, num_devices=1)
    arrays = {n: np.ascontiguousarray(a) for n, a in inputs.items()}
    arrays["W_top1"] = laid_w1(arrays["W_top1"])
    arrays["ids_small"] = np.ascontiguousarray(
        arrays["ids"][:, ONEHOT].reshape(TILE, TILES, len(ONEHOT)).transpose(2, 1, 0)[:, 1:].reshape(len(ONEHOT), LOOKED_UP))
    ap = {n: nc.dram_tensor(n, a.shape, mybir.dt.from_np(a.dtype), kind="ExternalInput").ap() for n, a in arrays.items()}
    out = nc.dram_tensor("y_out", (BATCH, 1), mybir.dt.float32, kind="ExternalOutput").ap()
    dlrm(nc, ap["r_dense_features"], ap["ids"], ap["ids_small"], [ap[f"tbl_{i}"] for i in range(TABLES)], ap["W_top1"],
         ap["b_top1"], ap["W_top2"], ap["b_top2"], ap["W_top3"], out)
    r = run_bass_kernel_spmd(nc, [arrays], core_ids=[0])
    return r.results[0]["y_out"]
```

```python
import concourse.bass as bass
from concourse import mybir
from contextlib import ExitStack
import numpy as np

BATCH, DIM = 512, 128
TABLES = 26
SLOTS = TABLES + 1
HIDDEN1, HIDDEN2 = 512, 256
H1, H2 = HIDDEN1 // 128, HIDDEN2 // 128
TILE = 128
TILES = BATCH // TILE
QUAD = 32

SMALL, CHUNKS = 1000, 8
SMALL_P = SMALL // CHUNKS
SMALL_16 = SMALL_P // 16 * 16
ONEHOT = [2, 4, 5, 8, 13, 14, 16, 18, 22, 23, 25]
GATHERED = [i for i in range(TABLES) if i not in ONEHOT]
LOOKED_UP = BATCH - TILE
ID_PIECES = [range(0, 1)] + [range(k, min(k + 3, len(ONEHOT))) for k in range(1, len(ONEHOT), 3)]
RAW_BUFFERS = 3
CUT_BUFFERS = 2
PART_BUFFERS = 3
WARM_UP = 56
DVE_CHUNKS = 6
SLOT_FEATURE = [0] + [i + 1 for i in GATHERED + ONEHOT]
FIRST_ONEHOT = 1 + len(GATHERED)


def slot_groups(t):
    end = SLOTS if t == 0 else FIRST_ONEHOT
    return [list(range(s, min(s + 4, end))) for s in range(0, end, 4)]


TURNS = [(t, g) for t in range(TILES) for g in range(len(slot_groups(t)))]


def turns_through(t):
    return sum(1 for u, _ in TURNS if u <= t)


STEP = 7
RECTS = [(1, 0, 14, 14, 13), (1, 0, 7, 7, 7), (1, 14, 7, 21, 6), (3, 0, 3, 3, 4), (3, 0, 2, 1, 2),
         (3, 3, 3, 4, 3), (1, 21, 5, 22, 5)]
PACKED = sum(r[0] * r[2] * r[4] for r in RECTS)
NKT = -(-PACKED // 128)
KROWS = -(-PACKED // NKT)


def steps(text):
    return [(s.split()[0], *map(int, s.split()[1:])) for s in text.split(",")]


TENSOR_STEPS = steps("""
look 0, turn 0 0, look 1, turn 0 1, look 2, turn 0 2, look 3, turn 0 3, look 4, turn 0 4, look 5, turn 0 5,
turn 0 6, look 6, gram 0, look 7, turn 1 0, look 8, dense 0 0, dense 0 1, turn 1 1, pairs 0, turn 1 2,
turn 1 3, look 9, layer1 0, turn 2 0, look 10, layer2 0, gram 1, layer3 0, turn 2 1, turn 2 2, dense 1 0,
dense 1 1, pairs 1, turn 2 3, layer1 1, layer2 1, gram 2, turn 3 0, dense 2 0, dense 2 1, turn 3 1, layer3 1,
pairs 2, turn 3 2, turn 3 3, layer1 2, gram 3, layer2 2, dense 3 2, dense 3 3, pairs 3, layer3 2, dense 3 1,
dense 3 0, layer1 3, layer2 3, layer3 3""")
VECTOR_STEPS = steps("""
split 0, hot 0, hot 1, split 1, split 2, hot 2, split 3, split 4, hot 3, hot 4, split 5, hot 5, split 6,
hot 6, split 7, hot 7, split 8, hot 8, pack 0, split 9, hot 9, split 10, hot 10, pack 1, pack 2, pack 3""")
SCALAR_STEPS = steps("""
high 0, hot 0, hot 1, high 1, look 0, turn 0 0, hot 2, look 1, high 2, turn 0 1, high 3, hot 3, look 2,
turn 0 2, high 4, hot 4, look 3, hot 5, turn 0 3, high 5, look 4, hot 6, turn 0 4, high 6, look 5, turn 0 5,
high 7, turn 0 6, look 6, hot 7, high 8, hot 8, look 7, hot 9, high 9, turn 1 0, look 8, turn 1 1, pairs 0,
high 10, hot 10, turn 1 2, turn 1 3, look 9, layer1 0, turn 2 0, look 10, layer2 0, layer3 0, turn 2 1,
turn 2 2, pairs 1, turn 2 3, layer1 1, layer2 1, turn 3 0, turn 3 1, layer3 1, pairs 2, turn 3 2, turn 3 3,
layer1 2, layer2 2, pairs 3, layer3 2, layer1 3, layer2 3, layer3 3""")


def done_before(step, kind):
    return sum(1 for s in TENSOR_STEPS[:TENSOR_STEPS.index(step)] if s[0] == kind)


def dlrm(nc, dense, ids, ids_small, tables, w1, b1, w2, b2, w3, out):
    fp32, fp32r, i32 = mybir.dt.float32, mybir.dt.float32r, mybir.dt.int32
    ALU = mybir.AluOpType
    ACT = mybir.ActivationFunctionType
    NO = len(ONEHOT)
    WEIGHTS = 6 * 16
    ctx = ExitStack()
    with ctx:
        sb = lambda n, s, d=fp32: ctx.enter_context(nc.sbuf_tensor(n, s, d))
        pb = lambda n, s, d=fp32: ctx.enter_context(nc.psum_tensor(n, s, d))
        sem = lambda n: ctx.enter_context(nc.semaphore(n))
        ids_sb = sb("ids_sb", [128, TILES, TABLES], i32)
        idb = sb("idb", [128, NO, LOOKED_UP], i32)
        rowid = sb("rowid", [128, CHUNKS])
        rows = sb("rows", [128, 2, SLOTS, DIM])
        dense_sb = sb("dense_sb", [128, TILES, DIM])
        raw = sb("raw", [SMALL_P, RAW_BUFFERS, CHUNKS * DIM])
        cut = sb("cut", [SMALL_P, CUT_BUFFERS, CHUNKS * DIM])
        high = sb("high", [SMALL_P, PART_BUFFERS, CHUNKS * DIM], fp32r)
        low = sb("low", [SMALL_P, PART_BUFFERS, CHUNKS * DIM], fp32r)
        hot = sb("hot", [SMALL_P, PART_BUFFERS, CHUNKS, LOOKED_UP], fp32r)
        apart = sb("apart", [SMALL_P, CHUNKS - DVE_CHUNKS, LOOKED_UP])
        early = sb("early", [128, 1])
        ident = sb("ident", [128, 128])
        xT = sb("xT", [128, BATCH, SLOTS])
        gT = sb("gT", [128, SLOTS, QUAD])
        zc = sb("zc", [128, NKT * KROWS])
        zT = sb("zT", [KROWS, NKT, TILE])
        w1_sb = sb("w1_sb", [128, NKT + 1, HIDDEN1])
        w2_sb = sb("w2_sb", [128, H1, HIDDEN2])
        w3_sb = sb("w3_sb", [128, H2])
        b1_sb = sb("b1_sb", [128, H1])
        b2_sb = sb("b2_sb", [128, H2])
        h1 = sb("h1", [128, H1, TILE])
        h2 = sb("h2", [128, H2, TILE])
        y = sb("y", [128, TILES])
        ones = h2[:, 0, :]
        dense_w1_again = h1[:].rearrange("p n b -> p (n b)")
        turned_ps = pb("turned_ps", [128, 2, 4, 128])
        gram_ps = pb("gram_ps", [128, 2, 512])
        mlp_ps = pb("mlp_ps", [128, 2, 512])
        mlp2_ps = pb("mlp2_ps", [128, 512])
        shared_ps = pb("shared_ps", [128, 512])
        look_ps = shared_ps[:, 0:LOOKED_UP]
        pairs_ps = shared_ps[0:KROWS, 0:NKT * TILE].rearrange("p (k b) -> p k b", k=NKT)
        h2_ps = [mlp2_ps[:, 0:TILE], mlp_ps[:, 0, 2 * TILE:3 * TILE]]
        y_ps = mlp2_ps[:, TILE:TILE + 1]

        def h1_ps(t, n):
            if t < TILES - 1:
                return mlp_ps[:, n % 2, (n // 2) * TILE:(n // 2 + 1) * TILE]
            return mlp_ps[:, n, 0:TILE] if n < 2 else turned_ps[:, n - 2, 0, :]

        def dense_ahead(t):
            return 2 if t < TILES - 1 else H1

        s_ids = sem("ids_loaded")
        s_idb = [sem(f"ids_small_loaded{n}") for n in range(len(ID_PIECES))]
        s_dense = sem("dense_loaded")
        s_w = sem("weights_loaded")
        s_tbl = [sem(f"table_loaded{k}") for k in range(RAW_BUFFERS)]
        s_rows = [[sem(f"rows_gathered{t}_{g}") for g in range(len(slot_groups(0)))] for t in range(2)]
        s_rowid = sem("row_numbers_set")
        s_ones = sem("ones_set")
        s_ident = sem("identity_set")
        s_early = sem("functions_loaded")
        s_pg = sem("gram_psum_cleared")
        s_zpad = sem("pairs_padded")
        s_wd = sem("dense_weights_added")
        s_cut = sem("table_cut")
        s_low = sem("low_ready")
        s_high = sem("high_ready")
        s_hot = sem("hot_ready_by_dve")
        s_apart = sem("row_distance_ready")
        s_hota = sem("hot_ready_by_act")
        s_look = sem("lookup_done")
        s_lookx = sem("lookup_copied")
        s_turn = sem("rows_turned")
        s_turnx = sem("turned_copied")
        s_gram = sem("gram_done")
        s_gt = sem("gram_turned")
        s_zc = sem("pairs_packed")
        s_pairs = sem("pairs_turned")
        s_pairsx = sem("pairs_copied")
        s_h1p = sem("layer1_done")
        s_h1 = sem("layer1_relu")
        s_h2p = sem("layer2_done")
        s_h2 = sem("layer2_relu")
        s_yp = sem("layer3_done")
        s_y = sem("y_copied")
        s_out = sem("out_stored")

        def rect_of(copies, a0, na, b0, nb):
            one = gT[:, a0:a0 + na, b0:b0 + nb]
            p, a, b = one.ap
            return bass.AP(one.tensor, one.offset, [p, [STEP * (QUAD + 1), copies], a, b])

        def load_small_ids(queue, n):
            k = slice(ID_PIECES[n].start, ID_PIECES[n].stop)
            some = ids_small[k].rearrange("(o k) b -> o k b", o=1)
            queue.dma_start(idb[:, k, :], some.to_broadcast([128, *some.shape[1:]])).then_inc(s_idb[n], 16)

        def piece_of(j):
            return [n for n in range(len(ID_PIECES)) if j in ID_PIECES[n]][0]

        def load_table(queue, k):
            table = tables[ONEHOT[k]].rearrange("(p c) d -> p (c d)", c=CHUNKS)
            queue.dma_start(raw[0:SMALL_16, k % RAW_BUFFERS, :], table[0:SMALL_16]).then_inc(s_tbl[k % RAW_BUFFERS], 16)
            queue.dma_start(raw[SMALL_16:SMALL_P, k % RAW_BUFFERS, :], table[SMALL_16:SMALL_P]).then_inc(s_tbl[k % RAW_BUFFERS], 16)
        block = ctx.enter_context(nc.Block())

        @block.sync
        def _(sp):
            sp.dma_start(ids_sb[:], ids.rearrange("(p t) f -> p t f", t=TILES)).then_inc(s_ids, 16)
            load_small_ids(sp, 0)
            load_small_ids(sp, 1)
            load_table(sp, 1)
            sp.dma_start(dense_sb[:], dense.rearrange("(p t) d -> p t d", t=TILES)).then_inc(s_dense, 16)
            for k in range(2, NO):
                if k in [piece.start - 1 for piece in ID_PIECES]:
                    load_small_ids(sp, piece_of(k + 1))
                if k >= RAW_BUFFERS:
                    sp.wait_ge(s_low, k - RAW_BUFFERS + 1)
                load_table(sp, k)
                if k == 4:
                    sp.dma_start(w1_sb[:], w1[:, 0:NKT + 1]).then_inc(s_w, 16)
                    sp.dma_start(dense_w1_again, w1[:, NKT + 1]).then_inc(s_w, 16)
                    sp.dma_start(w2_sb[:], w2.rearrange("(k p) n -> p k n", p=128)).then_inc(s_w, 16)
                    with nc.allow_non_contiguous_dma(reason="a column, or biases by output row: a few hundred elements"):
                        sp.dma_start(w3_sb[:], w3.rearrange("(k p) o -> p (k o)", p=128)).then_inc(s_w, 16)
                        sp.dma_start(b1_sb[:], b1.rearrange("(k p) -> p k", p=128)).then_inc(s_w, 16)
                        sp.dma_start(b2_sb[:], b2.rearrange("(k p) -> p k", p=128)).then_inc(s_w, 16)
            sp.wait_ge(s_y, TILES)
            sp.dma_start(out.rearrange("(p t) o -> p (t o)", t=TILES), y[:]).then_inc(s_out, 16)
            sp.wait_ge(s_out, 16)

        @block.gpsimd
        def _(pool):
            pool.iota(rowid[:], pattern=[[1, CHUNKS]], base=0, channel_multiplier=CHUNKS,
                      allow_small_or_imprecise_dtypes=True).then_inc(s_rowid, 1)
            pool.memset(ones, 1.0).then_inc(s_ones, 1)
            pool.wait_ge(s_ones, 1)
            pool.affine_select(out=ident[:], in_=ones, compare_op=ALU.is_equal, fill=0.0, base=0,
                               pattern=[[-1, 128]], channel_multiplier=1).then_inc(s_ident, 1)
            pool.wait_ge(s_ids, 16)
            for t, g in TURNS:
                if t >= 2:
                    pool.wait_ge(s_turn, TURNS.index((t - 2, g)) + 1)
                for slot in slot_groups(t)[g]:
                    if slot:
                        i = SLOT_FEATURE[slot] - 1
                        pool.indirect_dma_start(
                            out=rows[:, t % 2, slot, :], out_offset=None, in_=tables[i],
                            in_offset=bass.IndirectOffsetOnAxis(ap=ids_sb[:, t, i:i + 1], axis=0)).then_inc(s_rows[t % 2][g], 16)

        @block.vector
        def _(dve):
            def split(k):
                dve.wait_ge(s_tbl[k % RAW_BUFFERS], 32 * (k // RAW_BUFFERS + 1))
                if k >= CUT_BUFFERS:
                    dve.wait_ge(s_high, k - CUT_BUFFERS + 1)
                if k >= PART_BUFFERS:
                    dve.wait_ge(s_look, k - PART_BUFFERS + 1)
                nc.vector.tensor_scalar(cut[:, k % CUT_BUFFERS, :].bitcast(i32), raw[:, k % RAW_BUFFERS, :].bitcast(i32), -4096, None,
                                        ALU.bitwise_and).then_inc(s_cut, 1)
                dve.wait_ge(s_cut, k + 1)
                nc.vector.tensor_sub(low[:, k % PART_BUFFERS, :], raw[:, k % RAW_BUFFERS, :], cut[:, k % CUT_BUFFERS, :]).then_inc(s_low, 1)

            def one_hot(j):
                if j == 0:
                    dve.wait_ge(s_rowid, 1)
                if j >= PART_BUFFERS:
                    dve.wait_ge(s_look, j - PART_BUFFERS + 1)
                dve.wait_ge(s_idb[piece_of(j)], 16)
                for c in range(DVE_CHUNKS):
                    last = nc.vector.tensor_scalar(hot[:, j % PART_BUFFERS, c, :], idb[0:SMALL_P, j, :],
                                                   rowid[0:SMALL_P, c:c + 1], None, ALU.is_equal)
                last.then_inc(s_hot, 1)

            def pack(t):
                if t == 0:
                    dve.wait_ge(s_w, WEIGHTS)
                    nc.vector.tensor_add(w1_sb[:, NKT, :], w1_sb[:, NKT, :], dense_w1_again).then_inc(s_wd, 1)
                dve.wait_ge(s_gram, t + 1)
                if t:
                    dve.wait_ge(s_pairs, t)
                    dve.wait_ge(s_zc, t)
                nc.vector.transpose(gT[:], gram_ps[:, :, 0:16 * SLOTS].rearrange("p h (m g) -> p g h m", g=SLOTS)).then_inc(s_gt, 1)
                dve.wait_ge(s_gt, t + 1)
                at = 0
                for rect in RECTS:
                    copies, _, na, _, nb = rect
                    size = copies * na * nb
                    last = nc.vector.tensor_copy(zc[:, at:at + size].rearrange("p (n a b) -> p n a b", n=copies, b=nb),
                                                 rect_of(*rect))
                    at += size
                last.then_inc(s_zc, 1)

            nc.vector.memset(gram_ps[:], 0.0).then_inc(s_pg, 1)
            nc.vector.memset(zc[:, PACKED:], 0.0).then_inc(s_zpad, 1)
            for step in VECTOR_STEPS:
                {"split": split, "hot": one_hot, "pack": pack}[step[0]](*step[1:])

        @block.scalar
        def _(act):
            def high_part(k):
                act.wait_ge(s_cut, k + 1)
                if k >= PART_BUFFERS:
                    act.wait_ge(s_look, k - PART_BUFFERS + 1)
                nc.scalar.copy(high[:, k % PART_BUFFERS, :], cut[:, k % CUT_BUFFERS, :]).then_inc(s_high, 1)

            def one_hot(j):
                if j == 0:
                    act.wait_ge(s_rowid, 1)
                act.wait_ge(s_idb[piece_of(j)], 16)
                if j:
                    act.wait_ge(s_hota, j)
                if j >= PART_BUFFERS:
                    act.wait_ge(s_look, j - PART_BUFFERS + 1)
                for c in range(DVE_CHUNKS, CHUNKS):
                    last = nc.scalar.activation(apart[:, c - DVE_CHUNKS, :], idb[0:SMALL_P, j, :], ACT.Abs,
                                                bias=rowid[0:SMALL_P, c:c + 1], scale=-1.0)
                last.then_inc(s_apart, 1)
                act.wait_ge(s_apart, j + 1)
                nc.scalar.activation(hot[:, j % PART_BUFFERS, DVE_CHUNKS:, :], apart[:], ACT.Relu, bias=1.0,
                                     scale=-1.0).then_inc(s_hota, 1)

            def copy_lookup(j):
                act.wait_ge(s_look, j + 1)
                nc.scalar.copy(xT[:, TILE:BATCH, FIRST_ONEHOT + j], look_ps).then_inc(s_lookx, 1)

            def copy_turned(t, g):
                turn = TURNS.index((t, g))
                first, n = slot_groups(t)[g][0], len(slot_groups(t)[g])
                act.wait_ge(s_turn, turn + 1)
                nc.scalar.copy(xT[:, t * TILE:(t + 1) * TILE, first:first + n],
                               turned_ps[:, turn % 2, 0:n, :].rearrange("p f b -> p b f")).then_inc(s_turnx, 1)

            def copy_pairs(t):
                act.wait_ge(s_pairs, t + 1)
                if t:
                    act.wait_ge(s_h1p, H1 * t)
                nc.scalar.copy(zT[:], pairs_ps).then_inc(s_pairsx, 1)

            def relu1(t):
                if t:
                    act.wait_ge(s_h2p, H2 * t)
                else:
                    act.wait_ge(s_w, WEIGHTS)
                for n in range(H1):
                    act.wait_ge(s_h1p, H1 * t + n + 1)
                    nc.scalar.activation(h1[:, n, :], h1_ps(t, n), ACT.Relu, bias=b1_sb[:, n:n + 1]).then_inc(s_h1, 1)

            def relu2(t):
                if t:
                    act.wait_ge(s_yp, t)
                for n in range(H2):
                    act.wait_ge(s_h2p, H2 * t + n + 1)
                    nc.scalar.activation(h2[:, n, :], h2_ps[n], ACT.Relu, bias=b2_sb[:, n:n + 1]).then_inc(s_h2, 1)

            def copy_y(t):
                act.wait_ge(s_yp, t + 1)
                nc.scalar.copy(y[:, t:t + 1], y_ps).then_inc(s_y, 1)

            load_table(act, 0)
            act.wait_ge(s_rowid, 1)
            nc.scalar.activation(early[:], rowid[:, 0:1], ACT.Abs).then_inc(s_early, 1)
            for step in SCALAR_STEPS:
                {"high": high_part, "hot": one_hot, "look": copy_lookup, "turn": copy_turned, "pairs": copy_pairs,
                 "layer1": relu1, "layer2": relu2, "layer3": copy_y}[step[0]](*step[1:])

        @block.tensor
        def _(pe):
            def lookup(j):
                pe.wait_ge(s_hot, j + 1)
                pe.wait_ge(s_hota, j + 1)
                pe.wait_ge(s_high, j + 1)
                if j:
                    pe.wait_ge(s_lookx, j)
                if done_before(("look", j), "pairs"):
                    pe.wait_ge(s_pairsx, done_before(("look", j), "pairs"))
                for part in (high, low):
                    if part is low:
                        pe.wait_ge(s_low, j + 1)
                    for c in range(CHUNKS):
                        last = nc.tensor.matmul(look_ps, part[:, j % PART_BUFFERS, c * DIM:(c + 1) * DIM], hot[:, j % PART_BUFFERS, c, :],
                                                start=part is high and c == 0, stop=part is low and c == CHUNKS - 1)
                last.then_inc(s_look, 1)

            def turn_rows(t, g):
                turn = TURNS.index((t, g))
                if turn == 0:
                    pe.wait_ge(s_dense, 16)
                gathered = sum(1 for u in range(t % 2, t + 1, 2) for slot in slot_groups(u)[g] if slot)
                pe.wait_ge(s_rows[t % 2][g], 16 * gathered)
                if turn >= 2:
                    pe.wait_ge(s_turnx, turn - 1)
                for i, slot in enumerate(slot_groups(t)[g]):
                    src = rows[:, t % 2, slot, :] if slot else dense_sb[:, t, :]
                    last = nc.tensor.transpose(turned_ps[:, turn % 2, i, :], src, ident[:])
                last.then_inc(s_turn, 1)

            def gram(t):
                pe.wait_ge(s_turnx, turns_through(t))
                if t == 0:
                    pe.wait_ge(s_pg, 1)
                else:
                    pe.wait_ge(s_lookx, NO)
                    pe.wait_ge(s_gt, t)
                for m in range(QUAD):
                    for q in range(4):
                        x = xT[:, t * TILE + QUAD * q + m, :]
                        c = (m % 16) * SLOTS
                        last = nc.tensor.matmul(gram_ps[QUAD * q:QUAD * q + SLOTS, m // 16, c:c + SLOTS], x, x, start=True, stop=True)
                last.then_inc(s_gram, 1)

            def turn_pairs(t):
                pe.wait_ge(s_zc, t + 1)
                if t:
                    pe.wait_ge(s_pairsx, t)
                else:
                    pe.wait_ge(s_zpad, 1)
                if done_before(("pairs", t), "look"):
                    pe.wait_ge(s_lookx, done_before(("pairs", t), "look"))
                for k in range(NKT):
                    last = nc.tensor.transpose(pairs_ps[:, k, :], zc[:, k * KROWS:(k + 1) * KROWS], ident[:])
                last.then_inc(s_pairs, 1)

            def dense_part(t, n):
                if t == 0:
                    pe.wait_ge(s_wd, 1)
                    pe.wait_ge(s_w, WEIGHTS)
                elif n < 2:
                    pe.wait_ge(s_h1, H1 * t)
                    if n == 0:
                        pe.wait_ge(s_h2, H2 * t)
                nc.tensor.matmul(h1_ps(t, n), w1_sb[:, NKT, n * 128:(n + 1) * 128], xT[:, t * TILE:(t + 1) * TILE, 0],
                                 start=True, stop=False)

            def layer1(t):
                pe.wait_ge(s_pairsx, t + 1)
                for n in range(H1):
                    c = slice(n * 128, (n + 1) * 128)
                    if n >= dense_ahead(t):
                        pe.wait_ge(s_h1, H1 * t + n - 1)
                        dense_part(t, n)
                    for k in range(NKT):
                        last = nc.tensor.matmul(h1_ps(t, n), w1_sb[0:KROWS, k, c], zT[:, k, :], start=False, stop=k == NKT - 1)
                    last.then_inc(s_h1p, 1)

            def layer2(t):
                if t:
                    pe.wait_ge(s_y, t)
                for n, blocks in [(0, range(H1 - 1)), (1, range(H1 - 1)), (0, [H1 - 1]), (1, [H1 - 1])]:
                    for k in blocks:
                        pe.wait_ge(s_h1, H1 * t + k + 1)
                        last = nc.tensor.matmul(h2_ps[n], w2_sb[:, k, n * 128:(n + 1) * 128], h1[:, k, :], start=k == 0,
                                                stop=k == H1 - 1)
                    if k == H1 - 1:
                        last.then_inc(s_h2p, 1)

            def layer3(t):
                for k in range(H2):
                    pe.wait_ge(s_h2, H2 * t + k + 1)
                    last = nc.tensor.matmul(y_ps, h2[:, k, :], w3_sb[:, k:k + 1], start=k == 0, stop=k == H2 - 1)
                last.then_inc(s_yp, 1)

            pe.wait_ge(s_ident, 1)
            for _ in range(WARM_UP):
                nc.tensor.transpose(turned_ps[:, 0, 0, :], ident[:], ident[:])
            for step in TENSOR_STEPS:
                {"look": lookup, "turn": turn_rows, "gram": gram, "pairs": turn_pairs, "dense": dense_part,
                 "layer1": layer1, "layer2": layer2, "layer3": layer3}[step[0]](*step[1:])


def laid_w1(w):
    first = [DIM]
    for f in range(SLOTS):
        first.append(first[f] + SLOTS - 1 - f)
    laid = np.zeros((NKT * KROWS, HIDDEN1), w.dtype)
    at = 0
    for copies, a0, na, b0, nb in RECTS:
        for k in range(copies):
            for a in range(a0 + k * STEP, a0 + k * STEP + na):
                for b in range(b0 + k * STEP, b0 + k * STEP + nb):
                    if a < b:
                        f, g = sorted((SLOT_FEATURE[a], SLOT_FEATURE[b]))
                        laid[at] = w[first[f] + g - f - 1]
                    at += 1
    tiles = np.zeros((128, NKT + 2, HIDDEN1), w.dtype)
    tiles[0:KROWS, 0:NKT] = laid.reshape(NKT, KROWS, HIDDEN1).transpose(1, 0, 2)
    tiles[:, NKT] = w[0:DIM]
    tiles[:, NKT + 1] = w[first[-1]:first[-1] + DIM]
    return tiles


def kernel(**inputs):
    import concourse.bacc as bacc
    from concourse.bass_utils import run_bass_kernel_spmd
    nc = bacc.Bacc("TRN2", target_bir_lowering=False, num_devices=1)
    arrays = {n: np.ascontiguousarray(a) for n, a in inputs.items()}
    arrays["W_top1"] = laid_w1(arrays["W_top1"])
    arrays["ids_small"] = np.ascontiguousarray(
        arrays["ids"][:, ONEHOT].reshape(TILE, TILES, len(ONEHOT)).transpose(2, 1, 0)[:, 1:].reshape(len(ONEHOT), LOOKED_UP))
    ap = {n: nc.dram_tensor(n, a.shape, mybir.dt.from_np(a.dtype), kind="ExternalInput").ap() for n, a in arrays.items()}
    out = nc.dram_tensor("y_out", (BATCH, 1), mybir.dt.float32, kind="ExternalOutput").ap()
    dlrm(nc, ap["r_dense_features"], ap["ids"], ap["ids_small"], [ap[f"tbl_{i}"] for i in range(TABLES)], ap["W_top1"],
         ap["b_top1"], ap["W_top2"], ap["b_top2"], ap["W_top3"], out)
    r = run_bass_kernel_spmd(nc, [arrays], core_ids=[0])
    return r.results[0]["y_out"]
```
